# Optimizing a Trainium2 kernel written in Bass

```python
import numpy as np
import jax
import jax.numpy as jnp

def _softmax(x, axis=-1):
    return jax.nn.softmax(x, axis=axis)

def _gelu(x):
    return jax.nn.gelu(x, approximate=True)

def _silu(x):
    return jax.nn.silu(x)

def _sigmoid(x):
    return jax.nn.sigmoid(x)

def _layernorm(x, axis=-1, eps=1e-05):
    m = jnp.mean(x, axis=axis, keepdims=True)
    v = jnp.var(x, axis=axis, keepdims=True)
    return (x - m) / jnp.sqrt(v + eps)

def _scatter_add(tgt, idx, src, axis=0):
    return tgt.at[idx].add(src)

def _segment_sum(src, seg, n):
    return jax.ops.segment_sum(src, seg, n)
kernel_name = 'mk_dlrm_tower_d1_rec_r8_61b547'

def setup_inputs(seed: int=0):
    np.random.seed(seed)
    _w = jnp.asarray

    def _rec_inputs():
        import jax
        import jax.numpy as jnp
        _tk = jax.random.key(seed)
        dense_ctx = jax.random.normal(jax.random.fold_in(_tk, 190), (2048, 16), jnp.float32)
        ids = jnp.stack([jax.random.randint(jax.random.fold_in(_tk, 200 + f), (2048,), 0, v, jnp.int32) for f, v in enumerate([12500, 1000, 12500, 12500, 12500, 1000, 1000, 1250, 12500, 12500, 125000, 12500, 125000, 12500, 12500, 1250, 125000, 12500, 1250, 12500, 12500, 125000, 1250, 1250, 125000, 1250, 1250, 1000, 125000, 12500, 1000, 1250, 1000, 12500, 1250, 1250, 12500, 1250, 1000, 12500])], axis=1)
        tbl_0 = 0.05 * jax.random.normal(jax.random.fold_in(_tk, 500 + 0), (12500, 32), jnp.float32)
        tbl_1 = 0.05 * jax.random.normal(jax.random.fold_in(_tk, 500 + 1), (1000, 32), jnp.float32)
        tbl_2 = 0.05 * jax.random.normal(jax.random.fold_in(_tk, 500 + 2), (12500, 32), jnp.float32)
        tbl_3 = 0.05 * jax.random.normal(jax.random.fold_in(_tk, 500 + 3), (12500, 32), jnp.float32)
        tbl_4 = 0.05 * jax.random.normal(jax.random.fold_in(_tk, 500 + 4), (12500, 32), jnp.float32)
        tbl_5 = 0.05 * jax.random.normal(jax.random.fold_in(_tk, 500 + 5), (1000, 32), jnp.float32)
        tbl_6 = 0.05 * jax.random.normal(jax.random.fold_in(_tk, 500 + 6), (1000, 32), jnp.float32)
        tbl_7 = 0.05 * jax.random.normal(jax.random.fold_in(_tk, 500 + 7), (1250, 32), jnp.float32)
        tbl_8 = 0.05 * jax.random.normal(jax.random.fold_in(_tk, 500 + 8), (12500, 32), jnp.float32)
        tbl_9 = 0.05 * jax.random.normal(jax.random.fold_in(_tk, 500 + 9), (12500, 32), jnp.float32)
        tbl_10 = 0.05 * jax.random.normal(jax.random.fold_in(_tk, 500 + 10), (125000, 32), jnp.float32)
        tbl_11 = 0.05 * jax.random.normal(jax.random.fold_in(_tk, 500 + 11), (12500, 32), jnp.float32)
        tbl_12 = 0.05 * jax.random.normal(jax.random.fold_in(_tk, 500 + 12), (125000, 32), jnp.float32)
        tbl_13 = 0.05 * jax.random.normal(jax.random.fold_in(_tk, 500 + 13), (12500, 32), jnp.float32)
        tbl_14 = 0.05 * jax.random.normal(jax.random.fold_in(_tk, 500 + 14), (12500, 32), jnp.float32)
        tbl_15 = 0.05 * jax.random.normal(jax.random.fold_in(_tk, 500 + 15), (1250, 32), jnp.float32)
        tbl_16 = 0.05 * jax.random.normal(jax.random.fold_in(_tk, 500 + 16), (125000, 32), jnp.float32)
        tbl_17 = 0.05 * jax.random.normal(jax.random.fold_in(_tk, 500 + 17), (12500, 32), jnp.float32)
        tbl_18 = 0.05 * jax.random.normal(jax.random.fold_in(_tk, 500 + 18), (1250, 32), jnp.float32)
        tbl_19 = 0.05 * jax.random.normal(jax.random.fold_in(_tk, 500 + 19), (12500, 32), jnp.float32)
        tbl_20 = 0.05 * jax.random.normal(jax.random.fold_in(_tk, 500 + 20), (12500, 32), jnp.float32)
        tbl_21 = 0.05 * jax.random.normal(jax.random.fold_in(_tk, 500 + 21), (125000, 32), jnp.float32)
        tbl_22 = 0.05 * jax.random.normal(jax.random.fold_in(_tk, 500 + 22), (1250, 32), jnp.float32)
        tbl_23 = 0.05 * jax.random.normal(jax.random.fold_in(_tk, 500 + 23), (1250, 32), jnp.float32)
        tbl_24 = 0.05 * jax.random.normal(jax.random.fold_in(_tk, 500 + 24), (125000, 32), jnp.float32)
        tbl_25 = 0.05 * jax.random.normal(jax.random.fold_in(_tk, 500 + 25), (1250, 32), jnp.float32)
        tbl_26 = 0.05 * jax.random.normal(jax.random.fold_in(_tk, 500 + 26), (1250, 32), jnp.float32)
        tbl_27 = 0.05 * jax.random.normal(jax.random.fold_in(_tk, 500 + 27), (1000, 32), jnp.float32)
        tbl_28 = 0.05 * jax.random.normal(jax.random.fold_in(_tk, 500 + 28), (125000, 32), jnp.float32)
        tbl_29 = 0.05 * jax.random.normal(jax.random.fold_in(_tk, 500 + 29), (12500, 32), jnp.float32)
        tbl_30 = 0.05 * jax.random.normal(jax.random.fold_in(_tk, 500 + 30), (1000, 32), jnp.float32)
        tbl_31 = 0.05 * jax.random.normal(jax.random.fold_in(_tk, 500 + 31), (1250, 32), jnp.float32)
        tbl_32 = 0.05 * jax.random.normal(jax.random.fold_in(_tk, 500 + 32), (1000, 32), jnp.float32)
        tbl_33 = 0.05 * jax.random.normal(jax.random.fold_in(_tk, 500 + 33), (12500, 32), jnp.float32)
        tbl_34 = 0.05 * jax.random.normal(jax.random.fold_in(_tk, 500 + 34), (1250, 32), jnp.float32)
        tbl_35 = 0.05 * jax.random.normal(jax.random.fold_in(_tk, 500 + 35), (1250, 32), jnp.float32)
        tbl_36 = 0.05 * jax.random.normal(jax.random.fold_in(_tk, 500 + 36), (12500, 32), jnp.float32)
        tbl_37 = 0.05 * jax.random.normal(jax.random.fold_in(_tk, 500 + 37), (1250, 32), jnp.float32)
        tbl_38 = 0.05 * jax.random.normal(jax.random.fold_in(_tk, 500 + 38), (1000, 32), jnp.float32)
        tbl_39 = 0.05 * jax.random.normal(jax.random.fold_in(_tk, 500 + 39), (12500, 32), jnp.float32)
        _rk = jax.random.fold_in(_tk, 7)
        W_top1 = 0.0354441 * jax.random.normal(jax.random.fold_in(_tk, 801), (796, 512), jnp.float32)
        W_top2 = 0.0441942 * jax.random.normal(jax.random.fold_in(_tk, 802), (512, 256), jnp.float32)
        W_top3 = 0.0625 * jax.random.normal(jax.random.fold_in(_tk, 803), (256, 1), jnp.float32)
        b_top1 = jnp.zeros((512,), jnp.float32)
        b_top2 = jnp.zeros((256,), jnp.float32)
        return (dense_ctx, ids, tbl_0, tbl_1, tbl_2, tbl_3, tbl_4, tbl_5, tbl_6, tbl_7, tbl_8, tbl_9, tbl_10, tbl_11, tbl_12, tbl_13, tbl_14, tbl_15, tbl_16, tbl_17, tbl_18, tbl_19, tbl_20, tbl_21, tbl_22, tbl_23, tbl_24, tbl_25, tbl_26, tbl_27, tbl_28, tbl_29, tbl_30, tbl_31, tbl_32, tbl_33, tbl_34, tbl_35, tbl_36, tbl_37, tbl_38, tbl_39, W_top1, b_top1, W_top2, b_top2, W_top3)
    dense_ctx, ids, tbl_0, tbl_1, tbl_2, tbl_3, tbl_4, tbl_5, tbl_6, tbl_7, tbl_8, tbl_9, tbl_10, tbl_11, tbl_12, tbl_13, tbl_14, tbl_15, tbl_16, tbl_17, tbl_18, tbl_19, tbl_20, tbl_21, tbl_22, tbl_23, tbl_24, tbl_25, tbl_26, tbl_27, tbl_28, tbl_29, tbl_30, tbl_31, tbl_32, tbl_33, tbl_34, tbl_35, tbl_36, tbl_37, tbl_38, tbl_39, W_top1, b_top1, W_top2, b_top2, W_top3 = _rec_inputs()

    def _L0_rec_setup():
        import jax, jax.numpy as jnp
        import numpy as np
        NUM_FIELDS = 40
        _I_IDX, _J_IDX = np.triu_indices(NUM_FIELDS, k=1)
        key = jax.random.key(seed)
        k1, k2 = jax.random.split(key)
        batch, num_fields, embed_dim = (1024, NUM_FIELDS, 32)
        num_interactions = num_fields * (num_fields - 1) // 2
        embeddings = jax.random.normal(k1, (batch, num_fields, embed_dim), dtype=jnp.float32)
        W = jax.random.normal(k2, (num_interactions, embed_dim, embed_dim), dtype=jnp.float32)
        return {'embeddings': embeddings, 'W': W}
    _L0_rec_all = _L0_rec_setup()
    _L0_rec_in = {k: v for k, v in _L0_rec_all.items() if k in ('W',)}
    del _L0_rec_all
    return {'dense_ctx': dense_ctx, 'ids': ids, 'tbl_0': tbl_0, 'tbl_1': tbl_1, 'tbl_2': tbl_2, 'tbl_3': tbl_3, 'tbl_4': tbl_4, 'tbl_5': tbl_5, 'tbl_6': tbl_6, 'tbl_7': tbl_7, 'tbl_8': tbl_8, 'tbl_9': tbl_9, 'tbl_10': tbl_10, 'tbl_11': tbl_11, 'tbl_12': tbl_12, 'tbl_13': tbl_13, 'tbl_14': tbl_14, 'tbl_15': tbl_15, 'tbl_16': tbl_16, 'tbl_17': tbl_17, 'tbl_18': tbl_18, 'tbl_19': tbl_19, 'tbl_20': tbl_20, 'tbl_21': tbl_21, 'tbl_22': tbl_22, 'tbl_23': tbl_23, 'tbl_24': tbl_24, 'tbl_25': tbl_25, 'tbl_26': tbl_26, 'tbl_27': tbl_27, 'tbl_28': tbl_28, 'tbl_29': tbl_29, 'tbl_30': tbl_30, 'tbl_31': tbl_31, 'tbl_32': tbl_32, 'tbl_33': tbl_33, 'tbl_34': tbl_34, 'tbl_35': tbl_35, 'tbl_36': tbl_36, 'tbl_37': tbl_37, 'tbl_38': tbl_38, 'tbl_39': tbl_39, 'W_top1': W_top1, 'b_top1': b_top1, 'W_top2': W_top2, 'b_top2': b_top2, 'W_top3': W_top3, 'L0_rec_W': _L0_rec_in['W']}

def reference(dense_ctx, ids, tbl_0, tbl_1, tbl_2, tbl_3, tbl_4, tbl_5, tbl_6, tbl_7, tbl_8, tbl_9, tbl_10, tbl_11, tbl_12, tbl_13, tbl_14, tbl_15, tbl_16, tbl_17, tbl_18, tbl_19, tbl_20, tbl_21, tbl_22, tbl_23, tbl_24, tbl_25, tbl_26, tbl_27, tbl_28, tbl_29, tbl_30, tbl_31, tbl_32, tbl_33, tbl_34, tbl_35, tbl_36, tbl_37, tbl_38, tbl_39, W_top1, b_top1, W_top2, b_top2, W_top3, L0_rec_W):
    import jax
    import jax.numpy as jnp

    def _L0_rec_ref(embeddings, W):
        import jax, jax.numpy as jnp
        import numpy as np
        NUM_FIELDS = 40
        _I_IDX, _J_IDX = np.triu_indices(NUM_FIELDS, k=1)
        vi = embeddings[:, _I_IDX, :]
        vj = embeddings[:, _J_IDX, :]
        return jnp.einsum('bke,kef,bkf->bk', vi, W, vj)
    e = jnp.stack([tbl_0[ids[:, 0]], tbl_1[ids[:, 1]], tbl_2[ids[:, 2]], tbl_3[ids[:, 3]], tbl_4[ids[:, 4]], tbl_5[ids[:, 5]], tbl_6[ids[:, 6]], tbl_7[ids[:, 7]], tbl_8[ids[:, 8]], tbl_9[ids[:, 9]], tbl_10[ids[:, 10]], tbl_11[ids[:, 11]], tbl_12[ids[:, 12]], tbl_13[ids[:, 13]], tbl_14[ids[:, 14]], tbl_15[ids[:, 15]], tbl_16[ids[:, 16]], tbl_17[ids[:, 17]], tbl_18[ids[:, 18]], tbl_19[ids[:, 19]], tbl_20[ids[:, 20]], tbl_21[ids[:, 21]], tbl_22[ids[:, 22]], tbl_23[ids[:, 23]], tbl_24[ids[:, 24]], tbl_25[ids[:, 25]], tbl_26[ids[:, 26]], tbl_27[ids[:, 27]], tbl_28[ids[:, 28]], tbl_29[ids[:, 29]], tbl_30[ids[:, 30]], tbl_31[ids[:, 31]], tbl_32[ids[:, 32]], tbl_33[ids[:, 33]], tbl_34[ids[:, 34]], tbl_35[ids[:, 35]], tbl_36[ids[:, 36]], tbl_37[ids[:, 37]], tbl_38[ids[:, 38]], tbl_39[ids[:, 39]]], axis=1)
    z = _L0_rec_ref(e, L0_rec_W)
    z = z.reshape(z.shape[0], -1)
    h = jnp.concatenate([z, dense_ctx], axis=1)
    h = jnp.maximum(h @ W_top1 + b_top1, 0.0)
    h = jnp.maximum(h @ W_top2 + b_top2, 0.0)
    y = h @ W_top3
    return y

_drawn_inputs = setup_inputs


def setup_inputs(seed=0):
    import zlib

    import numpy as np

    out = dict(_drawn_inputs(seed))
    spreads = {'b_top1': (0.0, 0.1), 'b_top2': (0.0, 0.1)}
    factors = {}
    for name, (base, spread) in spreads.items():
        noise = np.random.default_rng([zlib.crc32(name.encode()), seed]).standard_normal(out[name].shape)
        drawn = base * np.exp(spread * noise) if base else spread * noise
        out[name] = jnp.asarray(drawn.astype(out[name].dtype))
    for name, factor in factors.items():
        out[name] = (out[name] * factor).astype(out[name].dtype)
    return out
```

```python
from contextlib import ExitStack

import numpy as np

import concourse.bass as bass
from concourse import mybir

F32 = mybir.dt.float32
F32R = mybir.dt.float32r
I32 = mybir.dt.int32
ALU = mybir.AluOpType
ACT = mybir.ActivationFunctionType

P = 128
FIELDS = 40
E = 32
PER = P // E
GROUPS = FIELDS // PER
NB = 256
TILES = NB // P
HALF = 2
QUADS = 4

UNITS = []
for _c in range(GROUPS):
    _n = PER * (_c + 1) - (1 if _c else 0)
    UNITS += [(_c, list(range(_s, min(_s + 4, _n)))) for _s in range(0, _n, 4)]
NU = len(UNITS)
UNIT_END = [sum(1 for c, _ in UNITS if c <= g) for g in range(GROUPS)]
BATCHES = (NU + 1) // 2
Z_SLOTS = E // PER
Z_BANKS = -(-BATCHES // Z_SLOTS)
ROW_SLOTS = 5
UNIT_START = [0] + UNIT_END[:-1]
LEAD = 8
AHEAD = sum(1 for u in UNIT_START if u < LEAD)
E_SLOTS = 5
H2_TILES = 2
TAIL = [("layer1", Z_BANKS - 1), ("layer2", 0), ("layer3", 0)]
TAIL_AT = [2, 4, 6]
assert AHEAD < E_SLOTS and GROUPS % E_SLOTS == 0
assert NU % 2 == 1 and GROUPS % 2 == 0 and GROUPS % ROW_SLOTS == 0 and Z_BANKS % 2 == 0
W_TILES = sum(PER * (c + 1) for c in range(GROUPS))
DENSE_AT = 16


def tile_of(c, i):
    return PER * c * (c + 1) // 2 + i


def steps_of(first, last):
    turns = {}
    for g in range(AHEAD, GROUPS + (0 if last else AHEAD)):
        start = UNIT_START[g] if g < GROUPS else NU + UNIT_START[g - GROUPS]
        turns.setdefault(start - LEAD, []).append(("turn", g))
    tails = {} if first else dict(zip(TAIL_AT, TAIL))
    steps, pending = [], []

    def red(b):
        steps.extend(pending)
        pending.clear()
        steps.append(("red", b))
        if b % Z_SLOTS == Z_SLOTS - 1 and b != BATCHES - 1:
            pending.append(("layer1", b // Z_SLOTS))

    for n in range(NU):
        steps += turns.get(n, [])
        steps.append(("gen", n))
        if n >= 3 and n % 2:
            red((n - 3) // 2)
        if n in tails:
            steps.append(tails[n])
    red(BATCHES - 2)
    red(BATCHES - 1)
    return steps


def misc_reads(steps, until):
    each = {"turn": 2, "layer2": H2_TILES, "layer3": 1}
    return sum(each.get(kind, 0) for kind, _ in steps[:steps.index(until)])


def tower_kernel(nc, ids, tables, w_lay, w1_lay, b1, w2, b2, w3, dense_t, ident_in, select_in, out):
    batch = ids.shape[0]
    chunks = batch // NB
    H1, H2 = w2.shape
    M1, M2 = H1 // P, H2 // P
    KB = 2 * Z_BANKS
    PIECE = 10 * P
    pieces = W_TILES * P // PIECE

    GATHER = 16 * PER * TILES
    STACK = 16 * QUADS
    MISC = 2 * GROUPS + M2 + 1
    assert M2 == H2_TILES

    spread = nc.dram_tensor("spread", [GROUPS, P, 2, NB], F32, kind="Internal").ap()
    spread_v = spread.rearrange("s (a e) h b -> s e a h b", e=E)
    ids_v = ids.rearrange("(k t p) f -> k p t f", t=TILES, p=P)
    out_v = out.rearrange("(k b) o -> k o b", b=NB)
    dense_v = dense_t.rearrange("d (k b) -> k d b", b=NB)

    with ExitStack() as ctx:
        def sb(name, shape, dt=F32):
            return ctx.enter_context(nc.sbuf_tensor(name, shape, dt))

        def ps(name, shape):
            return ctx.enter_context(nc.psum_tensor(name, shape, F32))

        def sem(name):
            return ctx.enter_context(nc.semaphore(name))

        w_stack = sb("w_stack", [P, W_TILES * P], F32R)
        v_stack = sb("v_stack", [P, FIELDS - 1, NB], F32R)
        idx = sb("idx", [P, TILES, FIELDS], I32)
        rows = sb("rows", [P, ROW_SLOTS, TILES, P])
        e_t = sb("e_t", [P, E_SLOTS, NB])
        parts = sb("parts", [P, 2, 2, NB], F32R)
        prod = sb("prod", [P, 3, 4 * NB])
        w1_sb = sb("w1_sb", [P, KB, H1])
        w2_sb = sb("w2_sb", [P, M1, H2])
        w3_sb = sb("w3_sb", [P, M2])
        b1_sb = sb("b1_sb", [P, M1])
        b2_sb = sb("b2_sb", [P, M2])
        ident = sb("ident", [P, P])
        select = sb("select", [P, Z_SLOTS, E])
        late = sb("late", [P, 2 * PIECE])
        z_sb = late[:, 0:4 * NB].rearrange("p (s b) -> p s b", s=2)
        h1_sb = late[:, 4 * NB:(4 + M1) * NB].rearrange("p (m b) -> p m b", m=M1)
        y_sb = h1_sb[0:1, 0, :]
        h2_sb = late[:, (4 + M1) * NB:(4 + M1 + M2) * NB].rearrange("p (m b) -> p m b", m=M2)

        t_ps = ps("t_ps", [P, 2, 4 * NB])
        z_ps = ps("z_ps", [P, HALF * NB])
        h1_ps = ps("h1_ps", [P, M1, NB])
        misc_ps = ps("misc_ps", [P, 2 * NB])

        w_loaded = [sem(f"w_loaded{b}") for b in range(2)]
        w_rounded = sem("w_rounded")
        w_split = sem("w_split")
        consts = sem("consts")
        idx_loaded = [sem(f"idx_loaded{c}") for c in range(GROUPS)]
        gathered = [sem(f"gathered{c}") for c in range(GROUPS)]
        group_begun = sem("group_begun")
        turned = sem("turned")
        misc_read = sem("misc_read")
        split_done = sem("split_done")
        spread_out = [sem(f"spread_out{b}") for b in range(2)]
        loads_begun = sem("loads_begun")
        stacked = [sem(f"stacked{c}") for c in range(GROUPS)]
        gen_done = sem("gen_done")
        mult_done = sem("mult_done")
        red_done = sem("red_done")
        z_read = sem("z_read")
        dense_loaded = sem("dense_loaded")
        layer1_done = sem("layer1_done")
        h1_ready = sem("h1_ready")
        layer2_done = sem("layer2_done")
        layer3_done = sem("layer3_done")
        stored = sem("stored")
        CONSTS = 16 * 7

        block = ctx.enter_context(nc.Block())

        def per_chunk(eng, body):
            body(0, steps_of(True, False))
            with eng.Fori(1, chunks - 1) as k:
                body(k, steps_of(False, False))
            body(chunks - 1, steps_of(False, True))

        def misc_start(k):
            return 2 * AHEAD if isinstance(k, int) and k == 0 else k * MISC + 2 * AHEAD - M2 - 1

        def after(eng, semaphore, count):
            if not (isinstance(count, int) and count <= 0):
                eng.wait_ge(semaphore, count)

        @block.sync
        def _(sp):
            for c in range(GROUPS):
                fs = slice(PER * c, PER * c + PER)
                sp.dma_start(idx[:, :, fs], ids_v[0, :, :, fs]).then_inc(idx_loaded[c], 16)

            def load_pieces(n):
                for b in range(2):
                    after(sp, w_split, 2 * n + b - 1)
                    for q in range(QUADS):
                        sp.dma_start(late[E * q:E * q + E, b * PIECE:(b + 1) * PIECE],
                                     w_lay[:, bass.ds((2 * n + b) * PIECE, PIECE)]).then_inc(w_loaded[b], 16)

            load_pieces(0)
            with sp.Fori(1, pieces // 2) as n:
                load_pieces(n)

            def store(k, g):
                sp.wait_ge(split_done, k * GROUPS + g + 1)
                sp.dma_start(spread[g % GROUPS], parts[:, g % 2, :, :].bitcast(F32)).then_inc(spread_out[g % 2], 16)

            def load(k, c, last):
                sp.wait_ge(spread_out[c % 2], (k * (GROUPS // 2) + c // 2 + 1) * 16)
                used = min(PER, FIELDS - 1 - PER * c)
                for q in range(QUADS):
                    sp.dma_start(v_stack[E * q:E * q + E, PER * c:PER * c + used, :].bitcast(F32),
                                 spread_v[c, :, 0:used, q % 2, :]).then_inc(stacked[c], 16)
                if not last:
                    sp.wait_ge(gathered[c], (k + 1) * GATHER)
                    fs = slice(PER * c, PER * c + PER)
                    sp.dma_start(idx[:, :, fs], ids_v[k + 1, :, :, fs]).then_inc(idx_loaded[c], 16)

            def body(k, steps):
                last = ("turn", GROUPS) not in steps
                after(sp, gen_done, k * NU)
                sp.sem_inc(loads_begun, 1)
                for c in range(AHEAD):
                    load(k, c, last)
                for kind, g in steps:
                    if kind == "turn":
                        store(k, g)
                        if g < GROUPS:
                            load(k, g, last)

            for g in range(AHEAD):
                store(0, g)
            per_chunk(sp, body)

        @block.gpsimd
        def _(pool):
            def body(k, first):
                for c in range(GROUPS):
                    pool.wait_ge(idx_loaded[c], (k + 1) * 16)
                    if not first or c >= ROW_SLOTS:
                        pool.wait_ge(turned, k * GROUPS + c + 1 - ROW_SLOTS)
                    pool.sem_inc(group_begun, 1)
                    for f in range(PER * c, PER * c + PER):
                        for t in range(TILES):
                            pool.indirect_dma_start(
                                out=rows[:, c % ROW_SLOTS, t, E * (f % PER):E * (f % PER) + E], out_offset=None,
                                in_=tables[f],
                                in_offset=bass.IndirectOffsetOnAxis(ap=idx[:, t, f:f + 1], axis=0),
                            ).then_inc(gathered[c], 16)

            body(0, True)
            with pool.Fori(1, chunks) as k:
                body(k, False)

        @block.scalar
        def _(act):
            act.dma_start(ident[:, :], ident_in).then_inc(consts, 16)
            act.dma_start(select[:, :, :], select_in).then_inc(consts, 16)
            act.dma_start(b1_sb[:, :], b1).then_inc(consts, 16)
            act.dma_start(b2_sb[:, :], b2).then_inc(consts, 16)
            act.dma_start(w3_sb[:, :], w3).then_inc(consts, 16)
            act.dma_start(w2_sb[:, :, :], w2.rearrange("(m p) n -> p m n", p=P)).then_inc(consts, 16)
            act.dma_start(w1_sb[:, :, :], w1_lay).then_inc(consts, 16)
            with act.Fori(0, pieces // 2) as n:
                for b in range(2):
                    act.wait_ge(w_loaded[b], (n + 1) * 16 * QUADS)
                    nc.scalar.copy(w_stack[:, bass.ds((2 * n + b) * PIECE, PIECE)],
                                   late[:, b * PIECE:(b + 1) * PIECE]).then_inc(w_rounded, 1)
            act.wait_ge(consts, CONSTS)

            def turn(k, g):
                act.wait_ge(turned, k * GROUPS + g + 1)
                after(act, spread_out[g % 2], (k * (GROUPS // 2) + g // 2) * 16)
                before = g - E_SLOTS
                after(act, mult_done, k * NU + (UNIT_END[before] if before >= 0 else 0))
                nc.scalar.copy(parts[:, g % 2, 0, :], misc_ps[:, 0:NB]).then_inc(misc_read, 1)
                nc.scalar.copy(e_t[:, g % E_SLOTS, :], misc_ps[:, 0:NB]).then_inc(misc_read, 1)

            def tail(k, step, reads):
                if step[0] == "layer1":
                    act.wait_ge(layer1_done, (k + 1) * Z_BANKS)
                    after(act, stored, k * 16)
                    for m in range(M1):
                        nc.scalar.activation(h1_sb[:, m, :], h1_ps[:, m, :], ACT.Relu,
                                             bias=b1_sb[:, m:m + 1]).then_inc(h1_ready, 1)
                elif step[0] == "layer2":
                    act.wait_ge(layer2_done, k + 1)
                    for m in range(M2):
                        nc.scalar.activation(h2_sb[:, m, :], misc_ps[:, m * NB:(m + 1) * NB], ACT.Relu,
                                             bias=b2_sb[:, m:m + 1]).then_inc(misc_read, 1)
                else:
                    act.wait_ge(layer3_done, k + 1)
                    nc.scalar.copy(y_sb[:, :], misc_ps[0:1, 0:NB]).then_inc(misc_read, 1)
                    act.wait_ge(misc_read, reads + 1)
                    act.dma_start(out_v[k], y_sb[:, :]).then_inc(stored, 16)

            def body(k, steps):
                for step in steps:
                    kind, n = step
                    if kind == "turn":
                        turn(k, n)
                    elif kind == "red" and (n % Z_SLOTS == Z_SLOTS - 1 or n == BATCHES - 1):
                        zb = n // Z_SLOTS
                        act.wait_ge(red_done, k * NU + min(2 * n + 2, NU))
                        after(act, layer1_done, k * Z_BANKS + max(0, zb - 1))
                        if isinstance(k, int) and k == 0 and zb == 0:
                            act.wait_ge(w_split, pieces)
                        nc.scalar.copy(z_sb[:, zb % 2, :], z_ps[:, :]).then_inc(z_read, 1)
                        if zb == Z_BANKS - 1:
                            act.wait_ge(z_read, k * Z_BANKS + zb + 1)
                            act.dma_start(z_sb[DENSE_AT:DENSE_AT + dense_t.shape[0], zb % 2, NB:2 * NB],
                                          dense_v[k]).then_inc(dense_loaded, 16)
                    elif step in TAIL:
                        tail(k - 1, step, misc_start(k) + misc_reads(steps, step))

            for g in range(AHEAD):
                turn(0, g)
            per_chunk(act, body)
            for step in TAIL:
                tail(chunks - 1, step, misc_start(chunks) - 2 * AHEAD + misc_reads(TAIL, step))
            act.wait_ge(stored, chunks * 16)

        @block.vector
        def _(dve):
            with dve.Fori(0, pieces // 2) as n:
                for b in range(2):
                    dve.wait_ge(w_rounded, 2 * n + b + 1)
                    w_low = w_stack[P // 2:P, bass.ds((2 * n + b) * PIECE, PIECE)]
                    nc.vector.tensor_tensor(w_low, late[P // 2:P, b * PIECE:(b + 1) * PIECE],
                                            w_low.bitcast(F32), ALU.subtract).then_inc(w_split, 1)

            def lower_part(k, g, reads):
                dve.wait_ge(misc_read, reads + 2)
                nc.vector.tensor_tensor(parts[:, g % 2, 1, :], e_t[:, g % E_SLOTS, :],
                                        parts[:, g % 2, 0, :].bitcast(F32), ALU.subtract).then_inc(split_done, 1)

            def body(k, steps):
                due = []
                for step in steps:
                    kind, n = step
                    if kind == "turn":
                        due.append(step)
                    elif kind == "gen":
                        c, fields = UNITS[n]
                        cols = len(fields) * NB
                        dve.wait_ge(gen_done, k * NU + n + 1)
                        after(dve, red_done, k * NU + max(0, n - 2))
                        nc.vector.tensor_tensor(
                            prod[:, n % 3, 0:cols].rearrange("p (i b) -> p i b", b=NB),
                            t_ps[:, n % 2, 0:cols].rearrange("p (i b) -> p i b", b=NB),
                            e_t[:, c % E_SLOTS, :].unsqueeze(1).broadcast_to([P, len(fields), NB]),
                            ALU.mult).then_inc(mult_done, 1)
                        for turn in due:
                            lower_part(k, turn[1], misc_start(k) + misc_reads(steps, turn))
                        due.clear()

            for g in range(AHEAD):
                lower_part(0, g, 2 * g)
            per_chunk(dve, body)

        @block.tensor
        def _(pe):
            pe.wait_ge(consts, CONSTS)

            def turn(k, g, reads):
                pe.wait_ge(gathered[g % GROUPS], (k + 1 + g // GROUPS) * GATHER)
                after(pe, misc_read, reads)
                for t in range(TILES):
                    mm = nc.tensor.transpose(misc_ps[:, t * P:(t + 1) * P], rows[:, g % ROW_SLOTS, t, :], ident[:, :])
                mm.then_inc(turned, 1)

            def layer1(k, zb):
                pe.wait_ge(z_read, k * Z_BANKS + zb + 1)
                for half in range(2):
                    kb = 2 * zb + half
                    if kb == KB - 1:
                        pe.wait_ge(dense_loaded, (k + 1) * 16)
                    for m in range(M1):
                        mm = nc.tensor.matmul(h1_ps[:, m, :], w1_sb[:, kb, m * P:(m + 1) * P],
                                              z_sb[:, zb % 2, half * NB:(half + 1) * NB],
                                              start=(kb == 0 and m % 2 == 0), stop=(kb == KB - 1),
                                              skip_group_check=True)
                mm.then_inc(layer1_done, 1)

            def tail(k, step, reads):
                if step[0] == "layer1":
                    layer1(k, step[1])
                elif step[0] == "layer2":
                    pe.wait_ge(misc_read, reads)
                    pe.wait_ge(h1_ready, (k + 1) * M1)
                    for m in range(M2):
                        for j in range(M1):
                            mm = nc.tensor.matmul(misc_ps[:, m * NB:(m + 1) * NB],
                                                  w2_sb[:, j, m * P:(m + 1) * P], h1_sb[:, j, :],
                                                  start=(j == 0), stop=(j == M1 - 1))
                    mm.then_inc(layer2_done, 1)
                else:
                    pe.wait_ge(misc_read, reads)
                    for j in range(M2):
                        mm = nc.tensor.matmul(misc_ps[0:1, 0:NB], w3_sb[:, j:j + 1], h2_sb[:, j, :],
                                              start=(j == 0), stop=(j == M2 - 1))
                    mm.then_inc(layer3_done, 1)

            def body(k, steps):
                for step in steps:
                    kind, n = step
                    if kind == "turn":
                        turn(k, n, misc_start(k) + misc_reads(steps, step))
                    elif kind == "gen":
                        c, fields = UNITS[n]
                        if n == 0 or UNITS[n - 1][0] != c:
                            pe.wait_ge(stacked[c], (k + 1) * STACK)
                        after(pe, mult_done, k * NU + max(0, n - 1))
                        for a, i in enumerate(fields):
                            at = tile_of(c, i) * P
                            mm = nc.tensor.matmul(t_ps[:, n % 2, a * NB:(a + 1) * NB], w_stack[:, at:at + P],
                                                  v_stack[:, i, :], start=True, stop=True)
                        mm.then_inc(gen_done, 1)
                    elif kind == "red":
                        zb = n // Z_SLOTS
                        if n % Z_SLOTS == 0:
                            after(pe, z_read, k * Z_BANKS + zb)
                        units = range(2 * n, min(2 * n + 2, NU))
                        pe.wait_ge(mult_done, k * NU + units[-1] + 1)
                        for q in range(2 * len(units)):
                            u = units[q // 2]
                            cols = min(HALF * NB, len(UNITS[u][1]) * NB - (q % 2) * HALF * NB)
                            at = (q % 2) * HALF * NB
                            closes = n % Z_SLOTS == Z_SLOTS - 1 or n == BATCHES - (1 if q < 2 else 2)
                            mm = nc.tensor.matmul(z_ps[E * q:E * q + E, 0:cols], select[:, n % Z_SLOTS, :],
                                                  prod[:, u % 3, at:at + cols],
                                                  start=(n % Z_SLOTS == 0), stop=closes)
                            if q % 2:
                                mm.then_inc(red_done, 1)
                    elif step in TAIL:
                        tail(k - 1, step, misc_start(k) + misc_reads(steps, step))
                    else:
                        layer1(k, n)

            for g in range(AHEAD):
                turn(0, g, 2 * g)
            pe.wait_ge(w_split, pieces)
            per_chunk(pe, body)
            for step in TAIL:
                tail(chunks - 1, step, misc_start(chunks) - 2 * AHEAD + misc_reads(TAIL, step))


def kernel(**inputs):
    import concourse.bacc as bacc
    from concourse.bass_utils import run_bass_kernel_spmd

    nc = bacc.Bacc("TRN2", target_bir_lowering=False, num_devices=1)
    arrays = {}

    def give(name, a):
        a = np.ascontiguousarray(a)
        arrays[name] = a
        return nc.dram_tensor(name, a.shape, mybir.dt.from_np(a.dtype), kind="ExternalInput").ap()

    def pair(i, j):
        return i * FIELDS - i * (i + 1) // 2 + j - i - 1

    def columns(name):
        return np.asarray(inputs[name]).reshape(-1, P).T

    w = np.asarray(inputs["L0_rec_W"])
    w_lay = np.zeros((E, W_TILES, PER, E), w.dtype)
    w_top1 = np.asarray(inputs["W_top1"])
    w1_lay = np.zeros((P, 2 * Z_BANKS, w_top1.shape[1]), w_top1.dtype)
    for n, (c, fields) in enumerate(UNITS):
        for a, i in enumerate(fields):
            batch, q = n // 2, 2 * (n % 2) + a // HALF
            for jj in range(PER):
                j = PER * c + jj
                if j > i:
                    w_lay[:, tile_of(c, i), jj, :] = w[pair(i, j)]
                    row = E * q + PER * (batch % Z_SLOTS) + jj
                    w1_lay[row, 2 * (batch // Z_SLOTS) + a % HALF] = w_top1[pair(i, j)]
    pairs = w.shape[0]
    w1_lay[DENSE_AT:DENSE_AT + w_top1.shape[0] - pairs, -1] = w_top1[pairs:]

    select = np.zeros((P, Z_SLOTS, E), np.float32)
    for s in range(Z_SLOTS):
        for p in range(P):
            select[p, s, PER * s + p // E] = 1.0

    ids = give("ids", inputs["ids"])
    tables = [give(f"tbl_{f}", inputs[f"tbl_{f}"]) for f in range(FIELDS)]
    args = [
        give("w_lay", w_lay.reshape(E, -1)), give("w1_lay", w1_lay), give("b1_lay", columns("b_top1")),
        give("W_top2", inputs["W_top2"]), give("b2_lay", columns("b_top2")), give("w3_lay", columns("W_top3")),
        give("dense_t", np.asarray(inputs["dense_ctx"]).T), give("ident_lay", np.eye(P, dtype=np.float32)),
        give("select_lay", select),
    ]
    batch = inputs["ids"].shape[0]
    out = nc.dram_tensor("y", (batch, 1), F32, kind="ExternalOutput").ap()
    tower_kernel(nc, ids, tables, *args, out)
    r = run_bass_kernel_spmd(nc, [arrays], core_ids=[0])
    return r.results[0]["y"]
```

```python
from contextlib import ExitStack

import numpy as np

import concourse.bass as bass
from concourse import mybir

F32 = mybir.dt.float32
F32R = mybir.dt.float32r
I32 = mybir.dt.int32
ALU = mybir.AluOpType
ACT = mybir.ActivationFunctionType

P = 128
FIELDS = 40
E = 32
PER = P // E
GROUPS = FIELDS // PER
NB = 256
TILES = NB // P
HALF = 2
QUADS = 4

UNITS = []
for _c in range(GROUPS):
    _n = PER * (_c + 1) - (1 if _c else 0)
    UNITS += [(_c, list(range(_s, min(_s + 4, _n)))) for _s in range(0, _n, 4)]
_c, _fields = UNITS.pop()
UNITS += [(_c, _fields[:2]), (_c, _fields[2:])]
NU = len(UNITS)
UNIT_END = [sum(1 for c, _ in UNITS if c <= g) for g in range(GROUPS)]
BATCHES = NU // 2
Z_SLOTS = E // PER
Z_BANKS = -(-BATCHES // Z_SLOTS)
T_SLOTS = 2
PROD_SLOTS = 4
ROW_SLOTS = 5
E_SLOTS = 5
UNIT_START = [0] + UNIT_END[:-1]
LEAD = 8
AHEAD = sum(1 for u in UNIT_START if u < LEAD)
APART = 3
H1_TILES = 4
H2_TILES = 2
assert AHEAD < E_SLOTS and GROUPS % E_SLOTS == 0
assert NU % PROD_SLOTS == 0 and NU % T_SLOTS == 0
assert GROUPS % 2 == 0 and GROUPS % ROW_SLOTS == 0 and Z_BANKS % 2 == 0
GROUP_TILES = [PER * (c + 1) - (1 if c else 0) for c in range(GROUPS)]
W_TILES = sum(GROUP_TILES)
DENSE_AT = 16

LAYER1_PARTS = [(half, m) for half in range(2) for m in range(H1_TILES)]
LAYER2_PARTS = [(m, j) for m in range(H2_TILES) for j in range(H1_TILES)]
TAIL = ([("red", BATCHES - 1)] + [("layer1", Z_BANKS - 1, p) for p in range(len(LAYER1_PARTS))]
        + [("layer2", 0, p) for p in range(len(LAYER2_PARTS))] + [("layer3", 0)])
TAIL_AT = [1] + [2, 3, 3, 4, 5, 5, 6, 7] + [9, 9, 10, 10, 11, 11, 12, 12] + [15]

PIECE_TILES = 13
PIECE_SLOTS = 4
PIECES = -(-W_TILES // PIECE_TILES)
PIECES_TO_TURN = PIECES // AHEAD


def tile_of(c, i):
    return sum(GROUP_TILES[:c]) + i


def steps_of(first, last):
    at = {}
    for g in range(AHEAD, GROUPS):
        at.setdefault(UNIT_START[g] - LEAD, []).append(("turn", g))
    if not last:
        for g in range(AHEAD):
            at.setdefault(NU - 3 - APART * (AHEAD - 1 - g), []).append(("turn", GROUPS + g))
    steps, waiting = [], []
    for n in range(NU):
        steps += at.get(n, [])
        steps.append(("gen", n))
        if n >= 3 and n % 2:
            b = (n - 3) // 2
            steps.append(("red", b))
            if b % Z_SLOTS == Z_SLOTS - 1:
                bank_at = n
                waiting += [("layer1", b // Z_SLOTS, p) for p in range(len(LAYER1_PARTS))]
        ending = n >= NU - len(LAYER1_PARTS) // 2 - 1
        if waiting and n > bank_at + 1 and (n % 2 == 0 or ending):
            take = 2 if ending or len(waiting) == len(LAYER1_PARTS) else 1
            steps += waiting[:take]
            del waiting[:take]
        if not first:
            steps += [step for step, unit in zip(TAIL, TAIL_AT) if unit == n]
    assert not waiting
    return steps


def steps_before():
    steps = []
    for g in range(AHEAD):
        steps += [("split", p) for p in range(PIECES_TO_TURN * g, PIECES_TO_TURN * (g + 1))]
        steps.append(("turn", g))
    return steps + [("split", p) for p in range(PIECES_TO_TURN * AHEAD, PIECES)]


def misc_reads(steps, until):
    each = {("turn",): 2, ("layer2", len(LAYER2_PARTS) - 1): H2_TILES, ("layer3",): 1}
    return sum(each.get((s[0],) + s[2:], 0) for s in steps[:steps.index(until)])


def last_user(n, slots):
    return n - slots + 1


def ends_bank(b):
    return b % Z_SLOTS == Z_SLOTS - 1 or b == BATCHES - 1


def red_parts(b):
    def quadrants(b):
        return [(2 * s + h, 2 * b + s, h * HALF * NB, min(HALF, len(UNITS[2 * b + s][1]) - HALF * h) * NB)
                for s in range(2) for h in range(2) if len(UNITS[2 * b + s][1]) > HALF * h]

    rest = range(b + 1, min(BATCHES, (b // Z_SLOTS + 1) * Z_SLOTS))
    later = {q for other in rest for q, _, _, _ in quadrants(other)}
    return [part + (part[0] not in later,) for part in quadrants(b)]


def tower_kernel(nc, ids, tables, w_lay, w1_lay, b1, w2, b2, w3, dense_t, ident_in, select_in, out):
    batch = ids.shape[0]
    chunks = batch // NB
    H1, H2 = w2.shape
    M1, M2 = H1 // P, H2 // P
    KB = 2 * Z_BANKS

    GATHER = 16 * PER * TILES
    STACK = 16 * QUADS
    MISC = 2 * GROUPS + M2 + 1
    assert M1 == H1_TILES and M2 == H2_TILES

    spread = nc.dram_tensor("spread", [GROUPS, P, 2, NB], F32, kind="Internal").ap()
    spread_v = spread.rearrange("s (a e) h b -> s e a h b", e=E)
    ids_v = ids.rearrange("(k t p) f -> k p t f", t=TILES, p=P)
    out_v = out.rearrange("(k b) o -> k o b", b=NB)
    dense_v = dense_t.rearrange("d (k b) -> k d b", b=NB)

    with ExitStack() as ctx:
        def sb(name, shape, dt=F32):
            return ctx.enter_context(nc.sbuf_tensor(name, shape, dt))

        def ps(name, shape):
            return ctx.enter_context(nc.psum_tensor(name, shape, F32))

        def sem(name):
            return ctx.enter_context(nc.semaphore(name))

        w_stack = sb("w_stack", [P, W_TILES * P], F32R)
        v_stack = sb("v_stack", [P, FIELDS - 1, NB], F32R)
        idx = sb("idx", [P, TILES, FIELDS], I32)
        rows = sb("rows", [P, ROW_SLOTS, TILES, P])
        e_t = sb("e_t", [P, E_SLOTS, NB])
        parts = sb("parts", [P, 2, 2, NB], F32R)
        w1_sb = sb("w1_sb", [P, KB, H1])
        w2_sb = sb("w2_sb", [P, M1, H2])
        w3_sb = sb("w3_sb", [P, M2])
        b1_sb = sb("b1_sb", [P, M1])
        b2_sb = sb("b2_sb", [P, M2])
        ident = sb("ident", [P, P])
        select = sb("select", [P, Z_SLOTS, E])
        late = sb("late", [P, PIECE_SLOTS * PIECE_TILES * P])
        z_at, h1_at = PROD_SLOTS * 4 * NB, (PROD_SLOTS * 4 + 4) * NB
        h2_at, late_end = h1_at + M1 * NB, h1_at + (M1 + M2) * NB
        assert late_end <= late.shape[1]
        prod = late[:, 0:z_at].rearrange("p (s n) -> p s n", s=PROD_SLOTS)
        z_sb = late[:, z_at:h1_at].rearrange("p (s b) -> p s b", s=2)
        h1_sb = late[:, h1_at:h2_at].rearrange("p (m b) -> p m b", m=M1)
        y_sb = h1_sb[0:1, 0, :]
        h2_sb = late[:, h2_at:late_end].rearrange("p (m b) -> p m b", m=M2)

        t_ps = ps("t_ps", [P, T_SLOTS, 4 * NB])
        z_ps = ps("z_ps", [P, HALF * NB])
        h1_ps = ps("h1_ps", [P, M1, NB])
        misc_ps = ps("misc_ps", [P, 2 * NB])

        w_loaded = [sem(f"w_loaded{b}") for b in range(PIECE_SLOTS)]
        w_rounded = sem("w_rounded")
        w_split = sem("w_split")
        selects_loaded = sem("selects_loaded")
        consts = sem("consts")
        idx_loaded = [sem(f"idx_loaded{c}") for c in range(GROUPS)]
        gathered = [sem(f"gathered{c}") for c in range(GROUPS)]
        group_begun = sem("group_begun")
        turned = sem("turned")
        misc_read = sem("misc_read")
        split_done = sem("split_done")
        spread_out = [sem(f"spread_out{b}") for b in range(2)]
        loads_begun = sem("loads_begun")
        stacked = [sem(f"stacked{c}") for c in range(GROUPS)]
        gen_done = sem("gen_done")
        mult_done = sem("mult_done")
        red_done = sem("red_done")
        z_read = sem("z_read")
        dense_loaded = sem("dense_loaded")
        layer1_done = sem("layer1_done")
        h1_ready = sem("h1_ready")
        layer2_done = sem("layer2_done")
        layer3_done = sem("layer3_done")
        stored = sem("stored")
        CONSTS = 16 * 5

        block = ctx.enter_context(nc.Block())

        def per_chunk(eng, body):
            body(0, steps_of(True, False))
            with eng.Fori(1, chunks - 1) as k:
                body(k, steps_of(False, False))
            body(chunks - 1, steps_of(False, True))

        def misc_start(k):
            return 2 * AHEAD if isinstance(k, int) and k == 0 else k * MISC + 2 * AHEAD - M2 - 1

        def piece_of(p):
            start, end = PIECE_TILES * p * P, min(PIECE_TILES * (p + 1), W_TILES) * P
            at = p % PIECE_SLOTS * PIECE_TILES * P
            return slice(start, end), slice(at, at + end - start)

        def after(eng, semaphore, count):
            if not (isinstance(count, int) and count <= 0):
                eng.wait_ge(semaphore, count)

        @block.sync
        def _(sp):
            for c in range(GROUPS):
                fs = slice(PER * c, PER * c + PER)
                sp.dma_start(idx[:, :, fs], ids_v[0, :, :, fs]).then_inc(idx_loaded[c], 16)

            def load_w(p):
                cols, raw = piece_of(p)
                if p >= PIECE_SLOTS:
                    sp.wait_ge(w_split, p - PIECE_SLOTS + 1)
                for q in range(QUADS):
                    sp.dma_start(late[E * q:E * q + E, raw], w_lay[:, cols]).then_inc(w_loaded[p % PIECE_SLOTS], 16)

            def store(k, g):
                sp.wait_ge(split_done, k * GROUPS + g + 1)
                sp.dma_start(spread[g % GROUPS], parts[:, g % 2, :, :].bitcast(F32)).then_inc(spread_out[g % 2], 16)

            def load(k, c):
                if c < AHEAD:
                    after(sp, gen_done, k * NU - (NU - UNIT_START[GROUPS - 1] - c - 1))
                    sp.sem_inc(loads_begun, 1)
                sp.wait_ge(spread_out[c % 2], (k * (GROUPS // 2) + c // 2 + 1) * 16)
                used = min(PER, FIELDS - 1 - PER * c)
                for q in range(QUADS):
                    sp.dma_start(v_stack[E * q:E * q + E, PER * c:PER * c + used, :].bitcast(F32),
                                 spread_v[c, :, 0:used, q % 2, :]).then_inc(stacked[c], 16)

            def load_idx(k, c):
                sp.wait_ge(gathered[c], (k + 1) * GATHER)
                fs = slice(PER * c, PER * c + PER)
                sp.dma_start(idx[:, :, fs], ids_v[k + 1, :, :, fs]).then_inc(idx_loaded[c], 16)

            def body(k, steps):
                last = ("turn", GROUPS) not in steps
                if not last:
                    for c in range(AHEAD):
                        load_idx(k, c)
                for step in steps:
                    if step[0] == "turn":
                        g = step[1]
                        store(k, g)
                        load(k + g // GROUPS, g % GROUPS)
                        if g < GROUPS and not last:
                            load_idx(k, g)

            parts_due = []
            for kind, n in steps_before():
                if kind == "split":
                    load_w(n)
                    if parts_due and n % PIECES_TO_TURN == PIECES_TO_TURN - 1:
                        store(0, parts_due[0])
                        load(0, parts_due.pop(0))
                else:
                    parts_due.append(n)
            for g in parts_due:
                store(0, g)
                load(0, g)
            per_chunk(sp, body)

        @block.gpsimd
        def _(pool):
            def body(k, first):
                for c in range(GROUPS):
                    pool.wait_ge(idx_loaded[c], (k + 1) * 16)
                    if not first or c >= ROW_SLOTS:
                        pool.wait_ge(turned, k * GROUPS + c + 1 - ROW_SLOTS)
                    pool.sem_inc(group_begun, 1)
                    for f in range(PER * c, PER * c + PER):
                        for t in range(TILES):
                            pool.indirect_dma_start(
                                out=rows[:, c % ROW_SLOTS, t, E * (f % PER):E * (f % PER) + E], out_offset=None,
                                in_=tables[f],
                                in_offset=bass.IndirectOffsetOnAxis(ap=idx[:, t, f:f + 1], axis=0),
                            ).then_inc(gathered[c], 16)

            body(0, True)
            with pool.Fori(1, chunks) as k:
                body(k, False)

        @block.scalar
        def _(act):
            act.dma_start(ident[:, :], ident_in).then_inc(selects_loaded, 16)
            act.dma_start(select[:, :, :], select_in).then_inc(selects_loaded, 16)
            act.dma_start(b1_sb[:, :], b1).then_inc(consts, 16)
            act.dma_start(b2_sb[:, :], b2).then_inc(consts, 16)
            act.dma_start(w3_sb[:, :], w3).then_inc(consts, 16)
            act.dma_start(w2_sb[:, :, :], w2.rearrange("(m p) n -> p m n", p=P)).then_inc(consts, 16)
            act.dma_start(w1_sb[:, :, :], w1_lay).then_inc(consts, 16)

            def split_w(p):
                cols, raw = piece_of(p)
                act.wait_ge(w_loaded[p % PIECE_SLOTS], (p // PIECE_SLOTS + 1) * 16 * QUADS)
                nc.scalar.copy(w_stack[:, cols], late[:, raw]).then_inc(w_rounded, 1)

            def turn(k, g):
                act.wait_ge(turned, k * GROUPS + g + 1)
                after(act, spread_out[g % 2], (k * (GROUPS // 2) + g // 2) * 16)
                before = g - E_SLOTS
                after(act, mult_done, k * NU + (UNIT_END[before] if before >= 0 else 0))
                nc.scalar.copy(parts[:, g % 2, 0, :], misc_ps[:, 0:NB]).then_inc(misc_read, 1)
                nc.scalar.copy(e_t[:, g % E_SLOTS, :], misc_ps[:, 0:NB]).then_inc(misc_read, 1)

            def read_z(k, zb):
                act.wait_ge(red_done, k * BATCHES + min((zb + 1) * Z_SLOTS, BATCHES))
                after(act, layer1_done, k * Z_BANKS + zb - 1)
                if isinstance(k, int) and k == 0 and zb == 0:
                    act.wait_ge(w_split, PIECES)
                nc.scalar.copy(z_sb[:, zb % 2, :], z_ps[:, :]).then_inc(z_read, 1)
                if zb == Z_BANKS - 1:
                    act.wait_ge(z_read, k * Z_BANKS + zb + 1)
                    act.dma_start(z_sb[DENSE_AT:DENSE_AT + dense_t.shape[0], zb % 2, NB:2 * NB],
                                  dense_v[k]).then_inc(dense_loaded, 16)

            def tail(k, step, reads):
                if step[0] == "red":
                    read_z(k, Z_BANKS - 1)
                elif step[0] == "layer1" and step[2] == len(LAYER1_PARTS) - 1:
                    act.wait_ge(layer1_done, (k + 1) * Z_BANKS)
                    after(act, stored, k * 16)
                    for m in range(M1):
                        nc.scalar.activation(h1_sb[:, m, :], h1_ps[:, m, :], ACT.Relu,
                                             bias=b1_sb[:, m:m + 1]).then_inc(h1_ready, 1)
                elif step[0] == "layer2" and step[2] == len(LAYER2_PARTS) - 1:
                    act.wait_ge(layer2_done, k + 1)
                    for m in range(M2):
                        nc.scalar.activation(h2_sb[:, m, :], misc_ps[:, m * NB:(m + 1) * NB], ACT.Relu,
                                             bias=b2_sb[:, m:m + 1]).then_inc(misc_read, 1)
                elif step[0] == "layer3":
                    act.wait_ge(layer3_done, k + 1)
                    nc.scalar.copy(y_sb[:, :], misc_ps[0:1, 0:NB]).then_inc(misc_read, 1)
                    act.wait_ge(misc_read, reads + 1)
                    act.dma_start(out_v[k], y_sb[:, :]).then_inc(stored, 16)

            def body(k, steps):
                for step in steps:
                    if step[0] == "turn":
                        turn(k, step[1])
                    elif step in TAIL:
                        tail(k - 1, step, misc_start(k) + misc_reads(steps, step))
                    elif step[0] == "red" and ends_bank(step[1]):
                        read_z(k, step[1] // Z_SLOTS)

            for step in steps_before():
                if step[0] == "split":
                    split_w(step[1])
                else:
                    turn(0, step[1])
            act.wait_ge(consts, CONSTS)
            per_chunk(act, body)
            for step in TAIL:
                tail(chunks - 1, step, misc_start(chunks) - 2 * AHEAD + misc_reads(TAIL, step))
            act.wait_ge(stored, chunks * 16)

        @block.vector
        def _(dve):
            def split_w(p):
                cols, raw = piece_of(p)
                dve.wait_ge(w_rounded, p + 1)
                nc.vector.tensor_tensor(w_stack[P // 2:P, cols], late[P // 2:P, raw],
                                        w_stack[P // 2:P, cols].bitcast(F32), ALU.subtract).then_inc(w_split, 1)

            def lower_part(k, g, reads):
                dve.wait_ge(misc_read, reads + 2)
                nc.vector.tensor_tensor(parts[:, g % 2, 1, :], e_t[:, g % E_SLOTS, :],
                                        parts[:, g % 2, 0, :].bitcast(F32), ALU.subtract).then_inc(split_done, 1)

            def body(k, steps):
                due = []
                for step in steps:
                    if step[0] == "turn":
                        due.append(step)
                    elif step[0] == "gen":
                        n = step[1]
                        c, fields = UNITS[n]
                        cols = len(fields) * NB
                        dve.wait_ge(gen_done, k * NU + n + 1)
                        after(dve, red_done, k * BATCHES + n // 2 - PROD_SLOTS // 2 + 1)
                        nc.vector.tensor_tensor(
                            prod[:, n % PROD_SLOTS, 0:cols].rearrange("p (i b) -> p i b", b=NB),
                            t_ps[:, n % T_SLOTS, 0:cols].rearrange("p (i b) -> p i b", b=NB),
                            e_t[:, c % E_SLOTS, :].unsqueeze(1).broadcast_to([P, len(fields), NB]),
                            ALU.mult).then_inc(mult_done, 1)
                        for turn in due:
                            lower_part(k, turn[1], misc_start(k) + misc_reads(steps, turn))
                        due.clear()

            for step in steps_before():
                if step[0] == "split":
                    split_w(step[1])
                else:
                    lower_part(0, step[1], 2 * step[1])
            per_chunk(dve, body)

        @block.tensor
        def _(pe):
            pe.wait_ge(selects_loaded, 2 * 16)

            def turn(k, g, reads):
                pe.wait_ge(gathered[g % GROUPS], (k + 1 + g // GROUPS) * GATHER)
                after(pe, misc_read, reads)
                for t in range(TILES):
                    mm = nc.tensor.transpose(misc_ps[:, t * P:(t + 1) * P], rows[:, g % ROW_SLOTS, t, :], ident[:, :])
                mm.then_inc(turned, 1)

            def gen(k, n):
                c, fields = UNITS[n]
                if n == UNIT_START[c]:
                    pe.wait_ge(stacked[c], (k + 1) * STACK)
                after(pe, mult_done, k * NU + last_user(n, T_SLOTS))
                for a, i in enumerate(fields):
                    at = tile_of(c, i) * P
                    mm = nc.tensor.matmul(t_ps[:, n % T_SLOTS, a * NB:(a + 1) * NB], w_stack[:, at:at + P],
                                          v_stack[:, i, :], start=True, stop=True)
                mm.then_inc(gen_done, 1)

            def red(k, b):
                if b % Z_SLOTS == 0:
                    after(pe, z_read, k * Z_BANKS + b // Z_SLOTS)
                pe.wait_ge(mult_done, k * NU + 2 * b + 2)
                for q, u, at, cols, closes in red_parts(b):
                    mm = nc.tensor.matmul(z_ps[E * q:E * q + E, 0:cols], select[:, b % Z_SLOTS, :],
                                          prod[:, u % PROD_SLOTS, at:at + cols],
                                          start=(b % Z_SLOTS == 0), stop=closes)
                mm.then_inc(red_done, 1)

            def layer1(k, zb, part):
                half, m = LAYER1_PARTS[part]
                if part == 0:
                    pe.wait_ge(z_read, k * Z_BANKS + zb + 1)
                kb = 2 * zb + half
                if kb == KB - 1 and m == 0:
                    pe.wait_ge(dense_loaded, (k + 1) * 16)
                mm = nc.tensor.matmul(h1_ps[:, m, :], w1_sb[:, kb, m * P:(m + 1) * P],
                                      z_sb[:, zb % 2, half * NB:(half + 1) * NB],
                                      start=(kb == 0 and m % 2 == 0), stop=(kb == KB - 1),
                                      skip_group_check=True)
                if part == len(LAYER1_PARTS) - 1:
                    mm.then_inc(layer1_done, 1)

            def tail(k, step, reads):
                if step[0] == "red":
                    red(k, step[1])
                elif step[0] == "layer1":
                    layer1(k, step[1], step[2])
                elif step[0] == "layer2":
                    m, j = LAYER2_PARTS[step[2]]
                    if step[2] == 0:
                        pe.wait_ge(misc_read, reads)
                        pe.wait_ge(h1_ready, (k + 1) * M1)
                    mm = nc.tensor.matmul(misc_ps[:, m * NB:(m + 1) * NB],
                                          w2_sb[:, j, m * P:(m + 1) * P], h1_sb[:, j, :],
                                          start=(j == 0), stop=(j == M1 - 1))
                    if step[2] == len(LAYER2_PARTS) - 1:
                        mm.then_inc(layer2_done, 1)
                else:
                    pe.wait_ge(misc_read, reads)
                    for j in range(M2):
                        mm = nc.tensor.matmul(misc_ps[0:1, 0:NB], w3_sb[:, j:j + 1], h2_sb[:, j, :],
                                              start=(j == 0), stop=(j == M2 - 1))
                    mm.then_inc(layer3_done, 1)

            def body(k, steps):
                for step in steps:
                    if step[0] == "turn":
                        turn(k, step[1], misc_start(k) + misc_reads(steps, step))
                    elif step[0] == "gen":
                        gen(k, step[1])
                    elif step in TAIL:
                        tail(k - 1, step, misc_start(k) + misc_reads(steps, step))
                    elif step[0] == "red":
                        red(k, step[1])
                    elif step[0] == "layer1":
                        layer1(k, step[1], step[2])

            for g in range(AHEAD):
                turn(0, g, 2 * g)
            pe.wait_ge(consts, CONSTS)
            pe.wait_ge(w_split, PIECES)
            per_chunk(pe, body)
            for step in TAIL:
                tail(chunks - 1, step, misc_start(chunks) - 2 * AHEAD + misc_reads(TAIL, step))


def kernel(**inputs):
    import concourse.bacc as bacc
    from concourse.bass_utils import run_bass_kernel_spmd

    nc = bacc.Bacc("TRN2", target_bir_lowering=False, num_devices=1)
    arrays = {}

    def give(name, a):
        a = np.ascontiguousarray(a)
        arrays[name] = a
        return nc.dram_tensor(name, a.shape, mybir.dt.from_np(a.dtype), kind="ExternalInput").ap()

    def pair(i, j):
        return i * FIELDS - i * (i + 1) // 2 + j - i - 1

    def columns(name):
        return np.asarray(inputs[name]).reshape(-1, P).T

    w = np.asarray(inputs["L0_rec_W"])
    w_lay = np.zeros((E, W_TILES, PER, E), w.dtype)
    w_top1 = np.asarray(inputs["W_top1"])
    w1_lay = np.zeros((P, 2 * Z_BANKS, w_top1.shape[1]), w_top1.dtype)
    for n, (c, fields) in enumerate(UNITS):
        for a, i in enumerate(fields):
            batch, q = n // 2, 2 * (n % 2) + a // HALF
            for jj in range(PER):
                j = PER * c + jj
                if j > i:
                    w_lay[:, tile_of(c, i), jj, :] = w[pair(i, j)]
                    row = E * q + PER * (batch % Z_SLOTS) + jj
                    w1_lay[row, 2 * (batch // Z_SLOTS) + a % HALF] = w_top1[pair(i, j)]
    pairs = w.shape[0]
    w1_lay[DENSE_AT:DENSE_AT + w_top1.shape[0] - pairs, -1] = w_top1[pairs:]

    select = np.zeros((P, Z_SLOTS, E), np.float32)
    for s in range(Z_SLOTS):
        for p in range(P):
            select[p, s, PER * s + p // E] = 1.0

    ids = give("ids", inputs["ids"])
    tables = [give(f"tbl_{f}", inputs[f"tbl_{f}"]) for f in range(FIELDS)]
    args = [
        give("w_lay", w_lay.reshape(E, -1)), give("w1_lay", w1_lay), give("b1_lay", columns("b_top1")),
        give("W_top2", inputs["W_top2"]), give("b2_lay", columns("b_top2")), give("w3_lay", columns("W_top3")),
        give("dense_t", np.asarray(inputs["dense_ctx"]).T), give("ident_lay", np.eye(P, dtype=np.float32)),
        give("select_lay", select),
    ]
    batch = inputs["ids"].shape[0]
    out = nc.dram_tensor("y", (batch, 1), F32, kind="ExternalOutput").ap()
    tower_kernel(nc, ids, tables, *args, out)
    r = run_bass_kernel_spmd(nc, [arrays], core_ids=[0])
    return r.results[0]["y"]
```

```python
from contextlib import ExitStack

import numpy as np

import concourse.bass as bass
from concourse import mybir

F32 = mybir.dt.float32
F32R = mybir.dt.float32r
I32 = mybir.dt.int32
BF16 = mybir.dt.bfloat16
F16 = mybir.dt.float16
ALU = mybir.AluOpType
ACT = mybir.ActivationFunctionType

P = 128
FIELDS = 40
E = 32
PER = P // E
GROUPS = FIELDS // PER
NB = 256
TILES = NB // P
HALF = 2
QUADS = 4

UNITS = []
for _c in range(GROUPS):
    _n = PER * (_c + 1) - (1 if _c else 0)
    UNITS += [(_c, list(range(_s, min(_s + 4, _n)))) for _s in range(0, _n, 4)]
_c, _fields = UNITS.pop()
UNITS += [(_c, _fields[:2]), (_c, _fields[2:])]
NU = len(UNITS)
UNIT_END = [sum(1 for c, _ in UNITS if c <= g) for g in range(GROUPS)]
BATCHES = NU // 2
Z_SLOTS = E // PER
Z_BANKS = -(-BATCHES // Z_SLOTS)
T_SLOTS = 2
PROD_SLOTS = 4
HOT = 8
GATHERED = [g for g in range(GROUPS) if g != HOT]
ROW_SLOTS = 9
E_SLOTS = 5
UNIT_START = [0] + UNIT_END[:-1]
LEAD = 8
AHEAD = sum(1 for u in UNIT_START if u < LEAD)
APART = 3
H1_TILES = 4
H2_TILES = 2
assert AHEAD < E_SLOTS and GROUPS % E_SLOTS == 0
assert NU % PROD_SLOTS == 0 and NU % T_SLOTS == 0
assert GROUPS % 2 == 0 and len(GATHERED) * TILES % ROW_SLOTS == 0 and Z_BANKS % 2 == 0
GROUP_TILES = [PER * (c + 1) - (1 if c else 0) for c in range(GROUPS)]
W_TILES = sum(GROUP_TILES)

KB = 2 * Z_BANKS - 1
LAST_BANK = BATCHES - (Z_BANKS - 1) * Z_SLOTS
assert HALF * LAST_BANK == Z_SLOTS
DENSE_AT = [E * q + E - 2 * PER for q in (1, 3)]
DENSE_ROWS = 2 * PER
assert [len(fields) for _, fields in UNITS[-2:]] == [2, 1]

LAYER1_PARTS = [[(half, m) for half in range(2 if zb < Z_BANKS - 1 else 1) for m in range(H1_TILES)]
                for zb in range(Z_BANKS)]
LAYER2_PARTS = [(m, j) for m in range(H2_TILES) for j in range(H1_TILES)]
LAYER1_STEPS = [("layer1", zb, p) for zb in range(Z_BANKS) for p in range(len(LAYER1_PARTS[zb]))]
LAYER1_AT = [29, 30, 31, 33, 34, 35, 36, 38] + [39, 41, 42, 43, 45, 46, 48, 49] + [52, 53, 54, 55]
TAIL = ([("red", BATCHES - 1)] + LAYER1_STEPS[len(LAYER1_AT):]
        + [("layer2", 0, p) for p in range(len(LAYER2_PARTS))] + [("layer3", 0)])
TAIL_AT = [1] + [0, 2, 2, 3, 4, 4, 5, 6] + [9, 9, 10, 11, 12, 12, 13, 14] + [16]
assert len(TAIL) == len(TAIL_AT)

BLOCKS = 8
HOT_SLOTS = 2
TABLE_PARTS = 3
IDS_AT = 15
ONE_HOT_AT = UNIT_START[HOT] - LEAD - BLOCKS - 2

PIECE_TILES = 12
PIECE_SLOTS = 4
PIECES = -(-W_TILES // PIECE_TILES)
PIECES_TO_TURN = PIECES // AHEAD


def tile_of(c, i):
    return sum(GROUP_TILES[:c]) + i


def steps_of(first, last):
    at = {}
    for g in range(AHEAD, GROUPS):
        unit = UNIT_START[g] - LEAD
        at.setdefault(ONE_HOT_AT if g == HOT - 1 else unit, []).append(("turn", g))
    if not last:
        for g in range(AHEAD):
            at.setdefault(NU - 3 - APART * (AHEAD - 1 - g), []).append(("turn", GROUPS + g))
    steps = []
    for n in range(NU):
        steps += at.get(n, [])
        steps.append(("gen", n))
        if n >= 3 and n % 2:
            b = (n - 3) // 2
            steps.append(("red", b))
        steps += [step for step, unit in zip(LAYER1_STEPS, LAYER1_AT) if unit == n]
        if n == IDS_AT:
            steps.append(("hot_ids", 0))
        for unit, kind in ((n, "one_hot"), (n - 2, "lookup")):
            block = unit - ONE_HOT_AT
            if 0 <= block < BLOCKS:
                steps.append((kind, block))
        if not first:
            steps += [step for step, unit in zip(TAIL, TAIL_AT) if unit == n]
    return steps


def steps_before():
    steps = []
    for g in range(AHEAD):
        steps += [("split", p) for p in range(PIECES_TO_TURN * g, PIECES_TO_TURN * (g + 1))]
        steps.append(("turn", g))
    steps += [("split", p) for p in range(PIECES_TO_TURN * AHEAD, PIECES)]
    for stage in range(2):
        steps.insert(steps.index(("split", 2 * stage + 2)), ("tables", stage))
    return steps


def last_user(n, slots):
    return n - slots + 1


def ends_bank(b):
    return b % Z_SLOTS == Z_SLOTS - 1 or b == BATCHES - 1


def red_parts(b):
    def quadrants(b):
        cuts = [(0, HALF)] if b < BATCHES - LAST_BANK else [(h, 1) for h in range(HALF)]
        slot = b % Z_SLOTS * len(cuts)
        parts = []
        for n, (tile, tiles) in enumerate(cuts):
            for q in range(QUADS):
                u, a = 2 * b + q // 2, q % 2 * HALF + tile
                tiles_left = min(tiles, len(UNITS[u][1]) - a)
                if tiles_left > 0:
                    parts.append((q, slot + n, u, a * NB, tiles_left * NB, slot + n == 0))
        return parts

    rest = range(b + 1, min(BATCHES, (b // Z_SLOTS + 1) * Z_SLOTS))
    order = [part[0] for other in [b, *rest] for part in quadrants(other)]
    return [part + (part[0] not in order[n + 1:],) for n, part in enumerate(quadrants(b))]


def turns_until(g):
    return g // GROUPS * len(GATHERED) + GATHERED.index(g % GROUPS) + 1


def row_slot(g, t):
    return (GATHERED.index(g) * TILES + t) % ROW_SLOTS


def tower_kernel(nc, ids, tables, w_lay, w1_lay, b1, w2, b2, w3, dense_t, ident_in, select_in, hot_ids,
                 hot_tables, row_numbers, out):
    batch = ids.shape[0]
    chunks = batch // NB
    H1, H2 = w2.shape
    M1, M2 = H1 // P, H2 // P

    GATHER = 16 * PER * TILES
    STACK = 16 * QUADS
    assert M1 == H1_TILES and M2 == H2_TILES

    spread = nc.dram_tensor("spread", [GROUPS, P, 2, NB], F32, kind="Internal").ap()
    spread_v = spread.rearrange("s (a e) h b -> s e a h b", e=E)
    hot_ids_16 = nc.dram_tensor("hot_ids_16", [batch // NB, PER * NB], F16, kind="Internal").ap()
    ids_v = ids.rearrange("(k t p) f -> k p t f", t=TILES, p=P)
    out_v = out.rearrange("(k b) o -> k o b", b=NB)
    dense_v = dense_t.rearrange("d (k b) -> k d b", b=NB)

    with ExitStack() as ctx:
        def sb(name, shape, dt=F32):
            return ctx.enter_context(nc.sbuf_tensor(name, shape, dt))

        def ps(name, shape):
            return ctx.enter_context(nc.psum_tensor(name, shape, F32))

        def sem(name):
            return ctx.enter_context(nc.semaphore(name))

        w_stack = sb("w_stack", [P, W_TILES * P], F32R)
        v_stack = sb("v_stack", [P, FIELDS - 1, NB], F32R)
        idx = sb("idx", [P, TILES, FIELDS], I32)
        rows = sb("rows", [P, ROW_SLOTS, P])
        e_t = sb("e_t", [P, E_SLOTS, NB])
        parts = sb("parts", [P, 2, 2, NB], F32R)
        w1_sb = sb("w1_sb", [P, KB, H1])
        w2_sb = sb("w2_sb", [P, M1, H2])
        w3_sb = sb("w3_sb", [P, M2])
        b1_sb = sb("b1_sb", [P, M1])
        b2_sb = sb("b2_sb", [P, M2])
        ident = sb("ident", [P, P])
        select = sb("select", [P, 2 * E - PER])
        tables_16 = sb("tables_16", [P, BLOCKS, TABLE_PARTS, PER, E], BF16)
        row_number = sb("row_number", [P, BLOCKS])
        ids_raw = sb("ids_raw", [P, batch * PER // P], I32)
        ids_half = sb("ids_half", [P, batch * PER // P], F16)
        late = sb("late", [P, PIECE_SLOTS * PIECE_TILES * P])
        z_at = PROD_SLOTS * 4 * NB
        h1_at = z_at + 2 * HALF * NB
        late_end = h1_at + M1 * NB
        assert late_end <= late.shape[1]
        prod = late[:, 0:z_at].rearrange("p (s n) -> p s n", s=PROD_SLOTS)
        z_sb = late[:, z_at:h1_at].rearrange("p (s b) -> p s b", s=2)
        h1_sb = late[:, h1_at:late_end].rearrange("p (m b) -> p m b", m=M1)
        h2_sb = z_sb[:, 1, :].rearrange("p (m b) -> p m b", m=M2)
        y_sb = z_sb[0:1, 1, 0:NB]
        ids_sb = late[:, h1_at:h1_at + PER * NB // 2].bitcast(F16).rearrange("p (f b) -> p f b", f=PER)
        one_hot = [late[:, h1_at + PER * NB // 2:late_end].bitcast(BF16).rearrange("p (f b) -> p f b", f=PER),
                   z_sb[:, 1, :].bitcast(BF16).rearrange("p (f b) -> p f b", f=PER)]
        tables_raw = w1_sb[:, 0:2, :].rearrange("p k n -> p (k n)").rearrange("p (v f) -> p v f", v=BLOCKS)
        tables_rest = w1_sb[:, 2:4, :].rearrange("p k n -> p (k n)").rearrange("p (v f) -> p v f", v=BLOCKS)
        table_parts = tables_16.rearrange("p v s f e -> p s v (f e)")
        assert PER * E * BLOCKS == 2 * H1 and len(one_hot) == HOT_SLOTS

        t_ps = ps("t_ps", [P, T_SLOTS, 4 * NB])
        z_ps = ps("z_ps", [P, HALF * NB])
        h1_ps = ps("h1_ps", [P, M1, NB])
        h2_ps = h1_ps[:, 0:M2, :]
        y_ps = h1_ps[0:1, M2, :]
        e_ps = ps("e_ps", [P, NB])

        w_loaded = [sem(f"w_loaded{b}") for b in range(PIECE_SLOTS)]
        w_rounded = sem("w_rounded")
        w_split = sem("w_split")
        selects_loaded = sem("selects_loaded")
        consts = sem("consts")
        hot_loaded = sem("hot_loaded")
        table_copied = sem("table_copied")
        table_subtracted = sem("table_subtracted")
        ids_halved = sem("ids_halved")
        ids_kept = sem("ids_kept")
        hot_ids_loaded = sem("hot_ids_loaded")
        one_hot_made = sem("one_hot_made")
        looked_up = sem("looked_up")
        idx_begun = sem("idx_begun")
        idx_loaded = [sem(f"idx_loaded{c}") for c in range(GROUPS)]
        gathered = [sem(f"gathered{c}") for c in range(GROUPS)]
        group_begun = sem("group_begun")
        turned = sem("turned")
        e_read = sem("e_read")
        split_done = sem("split_done")
        spread_out = [sem(f"spread_out{b}") for b in range(2)]
        loads_begun = sem("loads_begun")
        stacked = [sem(f"stacked{c}") for c in range(GROUPS)]
        gen_done = sem("gen_done")
        mult_done = sem("mult_done")
        red_done = sem("red_done")
        z_read = sem("z_read")
        dense_loaded = sem("dense_loaded")
        layer1_done = sem("layer1_done")
        h1_ready = sem("h1_ready")
        layer2_done = sem("layer2_done")
        h2_ready = sem("h2_ready")
        layer3_done = sem("layer3_done")
        y_ready = sem("y_ready")
        stored = sem("stored")
        CONSTS = 16 * 5

        block = ctx.enter_context(nc.Block())

        def per_chunk(eng, body):
            body(0, steps_of(True, False))
            with eng.Fori(1, chunks - 1) as k:
                body(k, steps_of(False, False))
            body(chunks - 1, steps_of(False, True))

        def piece_of(p):
            start, end = PIECE_TILES * p * P, min(PIECE_TILES * (p + 1), W_TILES) * P
            at = p % PIECE_SLOTS * PIECE_TILES * P
            return slice(start, end), slice(at, at + end - start)

        def after(eng, semaphore, count):
            if not (isinstance(count, int) and count <= 0):
                eng.wait_ge(semaphore, count)

        @block.sync
        def _(sp):
            sp.dma_start(idx[:, :, :], ids_v[0]).then_inc(idx_begun, 16)

            def load_w(p):
                cols, raw = piece_of(p)
                if p >= PIECE_SLOTS:
                    sp.wait_ge(w_split, p - PIECE_SLOTS + 1)
                for q in range(QUADS):
                    sp.dma_start(late[E * q:E * q + E, raw], w_lay[:, cols]).then_inc(w_loaded[p % PIECE_SLOTS], 16)

            def store(k, g):
                sp.wait_ge(split_done, k * GROUPS + g + 1)
                sp.dma_start(spread[g % GROUPS], parts[:, g % 2, :, :].bitcast(F32)).then_inc(spread_out[g % 2], 16)

            def load(k, c):
                if c < AHEAD:
                    after(sp, gen_done, k * NU - (NU - UNIT_START[GROUPS - 1] - c - 1))
                    sp.sem_inc(loads_begun, 1)
                sp.wait_ge(spread_out[c % 2], (k * (GROUPS // 2) + c // 2 + 1) * 16)
                used = min(PER, FIELDS - 1 - PER * c)
                for q in range(QUADS):
                    sp.dma_start(v_stack[E * q:E * q + E, PER * c:PER * c + used, :].bitcast(F32),
                                 spread_v[c, :, 0:used, q % 2, :]).then_inc(stacked[c], 16)

            def load_idx(k, c):
                sp.wait_ge(gathered[c], (k + 1) * GATHER)
                fs = slice(PER * c, PER * c + PER)
                sp.dma_start(idx[:, :, fs], ids_v[k + 1, :, :, fs]).then_inc(idx_loaded[c], 16)

            def body(k, steps):
                last = ("turn", GROUPS) not in steps
                idx_due = list(range(AHEAD))
                for step in steps:
                    if step[0] == "turn":
                        g = step[1]
                        store(k, g)
                        load(k + g // GROUPS, g % GROUPS)
                        if g < GROUPS and not last:
                            for c in idx_due[:2] + [g] * (g != HOT):
                                load_idx(k, c)
                            del idx_due[:2]

            for p in range(PIECES):
                load_w(p)
                if p % PIECES_TO_TURN == 0 and p >= PIECES_TO_TURN + PIECE_SLOTS:
                    store(0, (p - PIECE_SLOTS) // PIECES_TO_TURN - 1)
            for g in range(AHEAD):
                if PIECES_TO_TURN * (g + 1) + PIECE_SLOTS >= PIECES:
                    store(0, g)
                else:
                    load(0, g)
            for g in range(AHEAD):
                if PIECES_TO_TURN * (g + 1) + PIECE_SLOTS >= PIECES:
                    load(0, g)
            per_chunk(sp, body)

        @block.gpsimd
        def _(pool):
            def body(k, first):
                waited = None
                for n, c in enumerate(GATHERED):
                    if first:
                        pool.wait_ge(idx_begun, 16)
                    else:
                        pool.wait_ge(idx_loaded[c], k * 16)
                    for t in range(TILES):
                        back = n * TILES + t - ROW_SLOTS
                        held = GATHERED[back // TILES] - (GROUPS if back < 0 else 0)
                        if held != waited and not (first and back < 0):
                            pool.wait_ge(turned, k * len(GATHERED) + turns_until(held))
                            waited = held
                        pool.sem_inc(group_begun, 1)
                        for f in range(PER):
                            pool.indirect_dma_start(
                                out=rows[:, row_slot(c, t), E * f:E * f + E], out_offset=None,
                                in_=tables[PER * c + f],
                                in_offset=bass.IndirectOffsetOnAxis(ap=idx[:, t, PER * c + f:PER * c + f + 1], axis=0),
                            ).then_inc(gathered[c], 16)

            body(0, True)
            with pool.Fori(1, chunks) as k:
                body(k, False)

        @block.scalar
        def _(act):
            act.dma_start(ident[:, :], ident_in).then_inc(selects_loaded, 16)
            act.dma_start(select[:, :], select_in).then_inc(selects_loaded, 16)
            act.dma_start(tables_raw, hot_tables).then_inc(hot_loaded, 16)
            act.dma_start(ids_raw[:, :], hot_ids).then_inc(hot_loaded, 16)
            act.dma_start(row_number[:, :], row_numbers).then_inc(hot_loaded, 16)

            def make_tables(stage):
                if stage == 0:
                    act.wait_ge(hot_loaded, 3 * 16)
                    nc.scalar.copy(table_parts[:, 0], tables_raw).then_inc(table_copied, 1)
                    nc.scalar.copy(ids_half[:, :], ids_raw[:, :]).then_inc(ids_halved, 1)
                    act.wait_ge(ids_halved, 1)
                    act.dma_start(hot_ids_16.rearrange("k n -> (k n)").rearrange("(p n) -> p n", p=P),
                                  ids_half[:, :]).then_inc(ids_kept, 16)
                else:
                    act.wait_ge(table_subtracted, 1)
                    nc.scalar.copy(table_parts[:, 1], tables_rest).then_inc(table_copied, 1)

            def split_w(p):
                cols, raw = piece_of(p)
                act.wait_ge(w_loaded[p % PIECE_SLOTS], (p // PIECE_SLOTS + 1) * 16 * QUADS)
                nc.scalar.copy(w_stack[:, cols], late[:, raw]).then_inc(w_rounded, 1)

            def turn(k, g):
                if g == HOT:
                    act.wait_ge(looked_up, (k + 1) * BLOCKS)
                else:
                    act.wait_ge(turned, k * len(GATHERED) + turns_until(g))
                after(act, spread_out[g % 2], (k * (GROUPS // 2) + g // 2) * 16)
                before = g - E_SLOTS
                after(act, mult_done, k * NU + (UNIT_END[before] if before >= 0 else 0))
                nc.scalar.copy(parts[:, g % 2, 0, :], e_ps[:, 0:NB]).then_inc(e_read, 1)
                nc.scalar.copy(e_t[:, g % E_SLOTS, :], e_ps[:, 0:NB]).then_inc(e_read, 1)

            def read_z(k, zb):
                act.wait_ge(red_done, k * BATCHES + min((zb + 1) * Z_SLOTS, BATCHES))
                after(act, layer1_done, k * Z_BANKS + zb - 1)
                if isinstance(k, int) and k == 0 and zb == 0:
                    act.wait_ge(w_split, PIECES)
                if zb == 1:
                    act.wait_ge(looked_up, (k + 1) * BLOCKS)
                    if isinstance(k, int) and k == 0:
                        act.wait_ge(consts, CONSTS)
                used = HALF * NB if zb < Z_BANKS - 1 else NB
                nc.scalar.copy(z_sb[:, zb % 2, 0:used], z_ps[:, 0:used]).then_inc(z_read, 1)
                if zb == Z_BANKS - 1:
                    act.wait_ge(z_read, k * Z_BANKS + zb + 1)
                    for n, at in enumerate(DENSE_AT):
                        act.dma_start(z_sb[at:at + DENSE_ROWS, zb % 2, 0:NB],
                                      dense_v[k, n * DENSE_ROWS:(n + 1) * DENSE_ROWS]).then_inc(dense_loaded, 16)

            def load_hot_ids(k):
                if isinstance(k, int) and k == 0:
                    act.wait_ge(ids_kept, 16)
                    act.wait_ge(w_split, PIECES)
                    act.wait_ge(table_subtracted, 2)
                    act.dma_start(w1_sb[:, :, :], w1_lay).then_inc(consts, 16)
                    act.dma_start(b1_sb[:, :], b1).then_inc(consts, 16)
                    act.dma_start(b2_sb[:, :], b2).then_inc(consts, 16)
                    act.dma_start(w3_sb[:, :], w3).then_inc(consts, 16)
                    act.dma_start(w2_sb[:, :, :], w2.rearrange("(m p) n -> p m n", p=P)).then_inc(consts, 16)
                else:
                    act.wait_ge(layer2_done, k)
                act.dma_start(ids_sb, hot_ids_16[k].unsqueeze(0).broadcast_to([P, PER * NB]).rearrange(
                    "p (f b) -> p f b", f=PER)).then_inc(hot_ids_loaded, 16)

            def tail(k, step):
                if step[0] == "red":
                    read_z(k, Z_BANKS - 1)
                elif step == LAYER1_STEPS[-1]:
                    act.wait_ge(layer1_done, (k + 1) * Z_BANKS)
                    act.wait_ge(looked_up, (k + 1) * BLOCKS)
                    for m in range(M1):
                        nc.scalar.activation(h1_sb[:, m, :], h1_ps[:, m, :], ACT.Relu,
                                             bias=b1_sb[:, m:m + 1]).then_inc(h1_ready, 1)
                elif step[0] == "layer2" and step[2] == len(LAYER2_PARTS) - 1:
                    act.wait_ge(layer2_done, k + 1)
                    for m in range(M2):
                        nc.scalar.activation(h2_sb[:, m, :], h2_ps[:, m, :], ACT.Relu,
                                             bias=b2_sb[:, m:m + 1]).then_inc(h2_ready, 1)
                elif step[0] == "layer3":
                    act.wait_ge(layer3_done, k + 1)
                    nc.scalar.copy(y_sb, y_ps).then_inc(y_ready, 1)
                    act.wait_ge(y_ready, k + 1)
                    act.dma_start(out_v[k], y_sb).then_inc(stored, 16)

            def body(k, steps):
                for step in steps:
                    if step[0] == "turn":
                        turn(k, step[1])
                    elif step[0] == "hot_ids":
                        load_hot_ids(k)
                    elif step in TAIL:
                        tail(k - 1, step)
                    elif step[0] == "red" and ends_bank(step[1]):
                        read_z(k, step[1] // Z_SLOTS)

            for step in steps_before():
                if step[0] == "split":
                    split_w(step[1])
                elif step[0] == "tables":
                    make_tables(step[1])
                else:
                    turn(0, step[1])
            per_chunk(act, body)
            for step in TAIL:
                tail(chunks - 1, step)
            act.wait_ge(stored, chunks * 16)

        @block.vector
        def _(dve):
            def split_w(p):
                cols, raw = piece_of(p)
                dve.wait_ge(w_rounded, p + 1)
                nc.vector.tensor_tensor(w_stack[P // 2:P, cols], late[P // 2:P, raw],
                                        w_stack[P // 2:P, cols].bitcast(F32), ALU.subtract).then_inc(w_split, 1)

            def lower_part(k, g):
                dve.wait_ge(e_read, 2 * (k * GROUPS + g + 1))
                nc.vector.tensor_tensor(parts[:, g % 2, 1, :], e_t[:, g % E_SLOTS, :],
                                        parts[:, g % 2, 0, :].bitcast(F32), ALU.subtract).then_inc(split_done, 1)

            def make_columns(k, n):
                if n == 0:
                    dve.wait_ge(hot_ids_loaded, (k + 1) * 16)
                if n == 1:
                    after(dve, stored, k * 16)
                after(dve, looked_up, k * BLOCKS + n - HOT_SLOTS + 1)
                nc.vector.tensor_scalar(one_hot[n % HOT_SLOTS], ids_sb, row_number[:, n:n + 1], None,
                                        op0=ALU.is_equal).then_inc(one_hot_made, 1)

            def body(k, steps):
                due = []
                for step in steps:
                    if step[0] == "turn":
                        due.append(step)
                    elif step[0] == "one_hot":
                        make_columns(k, step[1])
                    elif step[0] == "gen":
                        n = step[1]
                        c, fields = UNITS[n]
                        cols = len(fields) * NB
                        dve.wait_ge(gen_done, k * NU + n + 1)
                        after(dve, red_done, k * BATCHES + n // 2 - PROD_SLOTS // 2 + 1)
                        nc.vector.tensor_tensor(
                            prod[:, n % PROD_SLOTS, 0:cols].rearrange("p (i b) -> p i b", b=NB),
                            t_ps[:, n % T_SLOTS, 0:cols].rearrange("p (i b) -> p i b", b=NB),
                            e_t[:, c % E_SLOTS, :].unsqueeze(1).broadcast_to([P, len(fields), NB]),
                            ALU.mult).then_inc(mult_done, 1)
                        for turn in due:
                            lower_part(k, turn[1])
                        due.clear()

            def make_tables(stage):
                dve.wait_ge(table_copied, stage + 1)
                if stage == 0:
                    nc.vector.tensor_tensor(tables_rest, tables_raw, table_parts[:, 0],
                                            ALU.subtract).then_inc(table_subtracted, 1)
                else:
                    nc.vector.tensor_tensor(table_parts[:, 2], tables_rest, table_parts[:, 1],
                                            ALU.subtract).then_inc(table_subtracted, 1)

            for step in steps_before():
                if step[0] == "split":
                    split_w(step[1])
                elif step[0] == "tables":
                    make_tables(step[1])
                else:
                    lower_part(0, step[1])
            per_chunk(dve, body)

        @block.tensor
        def _(pe):
            pe.wait_ge(selects_loaded, 2 * 16)

            def turn(k, g):
                pe.wait_ge(gathered[g % GROUPS], (k + 1 + g // GROUPS) * GATHER)
                after(pe, e_read, 2 * (k * GROUPS + g))
                for t in range(TILES):
                    mm = nc.tensor.transpose(e_ps[:, t * P:(t + 1) * P], rows[:, row_slot(g % GROUPS, t), :], ident[:, :])
                mm.then_inc(turned, 1)

            def look_up(k, n):
                if n == 0:
                    pe.wait_ge(e_read, 2 * (k * GROUPS + HOT))
                pe.wait_ge(one_hot_made, k * BLOCKS + n + 1)
                for part in range(TABLE_PARTS):
                    for f in range(PER):
                        mm = nc.tensor.matmul(e_ps[E * f:E * f + E, :], tables_16[:, n, part, f, :],
                                              one_hot[n % HOT_SLOTS][:, f, :],
                                              start=(n == 0 and part == 0),
                                              stop=(n == BLOCKS - 1 and part == TABLE_PARTS - 1))
                mm.then_inc(looked_up, 1)

            def gen(k, n):
                c, fields = UNITS[n]
                if n == UNIT_START[c]:
                    pe.wait_ge(stacked[c], (k + 1) * STACK)
                after(pe, mult_done, k * NU + last_user(n, T_SLOTS))
                for a, i in enumerate(fields):
                    at = tile_of(c, i) * P
                    mm = nc.tensor.matmul(t_ps[:, n % T_SLOTS, a * NB:(a + 1) * NB], w_stack[:, at:at + P],
                                          v_stack[:, i, :], start=True, stop=True)
                mm.then_inc(gen_done, 1)

            def red(k, b):
                if b % Z_SLOTS == 0:
                    after(pe, z_read, k * Z_BANKS + b // Z_SLOTS)
                pe.wait_ge(mult_done, k * NU + 2 * b + 2)
                for q, s, u, at, cols, opens, closes in red_parts(b):
                    mm = nc.tensor.matmul(z_ps[E * q:E * q + E, 0:cols],
                                          select[:, E - PER - PER * s:2 * E - PER - PER * s],
                                          prod[:, u % PROD_SLOTS, at:at + cols],
                                          start=opens, stop=closes)
                mm.then_inc(red_done, 1)

            def layer1(k, zb, part):
                half, m = LAYER1_PARTS[zb][part]
                if zb == 0 and part == 0:
                    after(pe, y_ready, k)
                if isinstance(k, int) and k == 0 and zb == 0 and part == 0:
                    pe.wait_ge(consts, CONSTS)
                if part == 0:
                    pe.wait_ge(z_read, k * Z_BANKS + zb + 1)
                kb = 2 * zb + half
                if kb == KB - 1 and m == 0:
                    pe.wait_ge(dense_loaded, (k + 1) * 16 * len(DENSE_AT))
                mm = nc.tensor.matmul(h1_ps[:, m, :], w1_sb[:, kb, m * P:(m + 1) * P],
                                      z_sb[:, zb % 2, half * NB:(half + 1) * NB],
                                      start=(kb == 0 and m % 2 == 0), stop=(kb == KB - 1),
                                      skip_group_check=True)
                if part == len(LAYER1_PARTS[zb]) - 1:
                    mm.then_inc(layer1_done, 1)

            def tail(k, step):
                if step[0] == "red":
                    red(k, step[1])
                elif step[0] == "layer1":
                    layer1(k, step[1], step[2])
                elif step[0] == "layer2":
                    m, j = LAYER2_PARTS[step[2]]
                    if step[2] == 0:
                        pe.wait_ge(h1_ready, (k + 1) * M1)
                    mm = nc.tensor.matmul(h2_ps[:, m, :],
                                          w2_sb[:, j, m * P:(m + 1) * P], h1_sb[:, j, :],
                                          start=(m == 0 and j == 0), stop=(j == M1 - 1), skip_group_check=True)
                    if step[2] == len(LAYER2_PARTS) - 1:
                        mm.then_inc(layer2_done, 1)
                else:
                    pe.wait_ge(h2_ready, (k + 1) * M2)
                    for j in range(M2):
                        mm = nc.tensor.matmul(y_ps, w3_sb[:, j:j + 1], h2_sb[:, j, :],
                                              start=(j == 0), stop=(j == M2 - 1))
                    mm.then_inc(layer3_done, 1)

            def body(k, steps):
                for step in steps:
                    if step[0] == "turn":
                        if step[1] != HOT:
                            turn(k, step[1])
                    elif step[0] == "lookup":
                        look_up(k, step[1])
                    elif step[0] == "gen":
                        gen(k, step[1])
                    elif step in TAIL:
                        tail(k - 1, step)
                    elif step[0] == "red":
                        red(k, step[1])
                    elif step[0] == "layer1":
                        layer1(k, step[1], step[2])

            for g in range(AHEAD):
                turn(0, g)
            pe.wait_ge(w_split, PIECES)
            per_chunk(pe, body)
            for step in TAIL:
                tail(chunks - 1, step)


def kernel(**inputs):
    import concourse.bacc as bacc
    from concourse.bass_utils import run_bass_kernel_spmd

    nc = bacc.Bacc("TRN2", target_bir_lowering=False, num_devices=1)
    arrays = {}

    def give(name, a):
        a = np.ascontiguousarray(a)
        arrays[name] = a
        return nc.dram_tensor(name, a.shape, mybir.dt.from_np(a.dtype), kind="ExternalInput").ap()

    def pair(i, j):
        return i * FIELDS - i * (i + 1) // 2 + j - i - 1

    def columns(name):
        return np.asarray(inputs[name]).reshape(-1, P).T

    table_rows = [inputs[f"tbl_{f}"].shape[0] for f in range(FIELDS)]
    hot = sorted(sorted(range(FIELDS), key=lambda f: table_rows[f])[:PER])
    order = [f for f in range(FIELDS) if f not in hot]
    order[PER * HOT:PER * HOT] = hot
    assert max(table_rows[f] for f in hot) <= BLOCKS * P

    w = np.asarray(inputs["L0_rec_W"])
    w_lay = np.zeros((E, W_TILES, PER, E), w.dtype)
    w_top1 = np.asarray(inputs["W_top1"])
    w1_lay = np.zeros((P, KB, w_top1.shape[1]), w_top1.dtype)
    for n, (c, fields) in enumerate(UNITS):
        for a, i in enumerate(fields):
            batch, q, half = n // 2, 2 * (n % 2) + a // HALF, a % HALF
            zb, slot = batch // Z_SLOTS, batch % Z_SLOTS
            if zb == Z_BANKS - 1:
                slot, half = 2 * slot + half, 0
            for jj in range(PER):
                j = PER * c + jj
                if j > i:
                    first, second = sorted((order[i], order[j]))
                    w_pair = w[pair(first, second)]
                    w_lay[:, tile_of(c, i), jj, :] = w_pair if first == order[i] else w_pair.T
                    w1_lay[E * q + PER * slot + jj, 2 * zb + half] = w_top1[pair(first, second)]
    pairs = w.shape[0]
    for n, at in enumerate(DENSE_AT):
        w1_lay[at:at + DENSE_ROWS, -1] = w_top1[pairs + n * DENSE_ROWS:pairs + (n + 1) * DENSE_ROWS]

    select = np.zeros((P, 2 * E - PER), np.float32)
    select[np.arange(P), E - PER + np.arange(P) // E] = 1.0

    ids_all = np.asarray(inputs["ids"])[:, order]
    hot_tables = np.zeros((P, BLOCKS, PER, E), np.asarray(inputs["tbl_0"]).dtype)
    for n, f in enumerate(hot):
        table = np.zeros((BLOCKS * P, E), hot_tables.dtype)
        table[:table_rows[f]] = np.asarray(inputs[f"tbl_{f}"])
        hot_tables[:, :, n, :] = table.reshape(BLOCKS, P, E).transpose(1, 0, 2)
    hot_ids = ids_all[:, PER * HOT:PER * HOT + PER].reshape(-1, NB, PER).transpose(0, 2, 1).reshape(P, -1)
    row_numbers = (np.arange(BLOCKS)[None, :] * P + np.arange(P)[:, None]).astype(np.float32)

    ids = give("ids", ids_all)
    tables = [None if f in hot else give(f"tbl_{f}", inputs[f"tbl_{f}"]) for f in order]
    args = [
        give("w_lay", w_lay.reshape(E, -1)), give("w1_lay", w1_lay), give("b1_lay", columns("b_top1")),
        give("W_top2", inputs["W_top2"]), give("b2_lay", columns("b_top2")), give("w3_lay", columns("W_top3")),
        give("dense_t", np.asarray(inputs["dense_ctx"]).T), give("ident_lay", np.eye(P, dtype=np.float32)),
        give("select_lay", select), give("hot_ids", hot_ids),
        give("hot_tables", hot_tables.reshape(P, BLOCKS, PER * E)), give("row_numbers", row_numbers),
    ]
    batch = inputs["ids"].shape[0]
    out = nc.dram_tensor("y", (batch, 1), F32, kind="ExternalOutput").ap()
    tower_kernel(nc, ids, tables, *args, out)
    r = run_bass_kernel_spmd(nc, [arrays], core_ids=[0])
    return r.results[0]["y"]
```
